# Optimizing a Trainium2 kernel written in Bass

```python
import numpy as np
import jax
import jax.numpy as jnp

def _softmax(x, axis=-1):
    return jax.nn.softmax(x, axis=axis)

def _gelu(x):
    return jax.nn.gelu(x, approximate=True)

def _silu(x):
    return jax.nn.silu(x)

def _sigmoid(x):
    return jax.nn.sigmoid(x)

def _layernorm(x, axis=-1, eps=1e-05):
    m = jnp.mean(x, axis=axis, keepdims=True)
    v = jnp.var(x, axis=axis, keepdims=True)
    return (x - m) / jnp.sqrt(v + eps)

def _scatter_add(tgt, idx, src, axis=0):
    return tgt.at[idx].add(src)

def _segment_sum(src, seg, n):
    return jax.ops.segment_sum(src, seg, n)
kernel_name = 'mk_gnn_preln_d4_gnn_r32_99e02f'

def setup_inputs(seed: int=0):
    np.random.seed(seed)
    _w = jnp.asarray

    def _rec_inputs():
        import jax
        import jax.numpy as jnp
        _gk = jax.random.key(seed)
        x = -0.0005121 + 1.001 * jax.random.normal(jax.random.fold_in(_gk, 1), (3125, 32), jnp.float32)
        src = jax.random.randint(jax.random.fold_in(_gk, 2), (100000,), 0, 3125, jnp.int32)
        dst = jnp.minimum((3125 * jax.random.uniform(jax.random.fold_in(_gk, 3), (100000,)) ** 2.0).astype(jnp.int32), 99999)
        _o = jnp.argsort(dst, stable=True)
        src = src[_o]
        dst = dst[_o]
        edge_attr_16 = -0.00019784 + 0.999804 * jax.random.normal(jax.random.fold_in(_gk, 12), (100000, 16), jnp.float32)
        edge_attr_4 = 0.000398945 + 1.00003 * jax.random.normal(jax.random.fold_in(_gk, 13), (100000, 4), jnp.float32)
        return (x, src, dst, edge_attr_16, edge_attr_4)
    x, src, dst, edge_attr_16, edge_attr_4 = _rec_inputs()

    def _L0_gnn_setup():
        import jax, jax.numpy as jnp
        import numpy as np
        N_NODES = 3125
        N_EDGES = 200000
        D = 32
        key = jax.random.key(seed)
        k1, k2, k3, k4 = jax.random.split(key, 4)
        x = jax.random.normal(k1, (N_NODES, D), dtype=jnp.float32)
        W = jax.random.normal(k2, (D, D), dtype=jnp.float32) / np.sqrt(D)
        b = jnp.zeros((D,), dtype=jnp.float32)
        src = jax.random.randint(k3, (N_EDGES,), 0, N_NODES, dtype=jnp.int32)
        dst = jax.random.randint(k4, (N_EDGES,), 0, N_NODES, dtype=jnp.int32)
        return {'x': x, 'W': W, 'b': b, 'src': src, 'dst': dst}
    _L0_gnn_all = _L0_gnn_setup()
    _L0_gnn_in = {k: v for k, v in _L0_gnn_all.items() if k in ('W', 'b')}
    del _L0_gnn_all

    def _L1_gnn_setup():
        import jax, jax.numpy as jnp
        import numpy as np
        N_ATOMS = 3125
        N_EDGES = 12500
        ATOM_DIM = 32
        BOND_DIM = 16
        key = jax.random.key(seed)
        k1, k2, k3, k4 = jax.random.split(key, 4)
        atom_features = jax.random.normal(k1, (N_ATOMS, ATOM_DIM), dtype=jnp.float32)
        bond_features = jax.random.normal(k2, (N_EDGES, BOND_DIM), dtype=jnp.float32)
        pair_indices = jax.random.randint(k3, (N_EDGES, 2), 0, N_ATOMS, dtype=jnp.int64)
        limit = np.sqrt(6.0 / (BOND_DIM + ATOM_DIM * ATOM_DIM)).astype(np.float32)
        kernel = jax.random.uniform(k4, (BOND_DIM, ATOM_DIM * ATOM_DIM), dtype=jnp.float32, minval=-limit, maxval=limit)
        bias = jnp.zeros((ATOM_DIM * ATOM_DIM,), dtype=jnp.float32)
        return {'atom_features': atom_features, 'bond_features': bond_features, 'pair_indices': pair_indices, 'kernel': kernel, 'bias': bias}
    _L1_gnn_all = _L1_gnn_setup()
    _L1_gnn_in = {k: v for k, v in _L1_gnn_all.items() if k in ('kernel', 'bias')}
    del _L1_gnn_all

    def _L2_gnn_setup():
        import jax, jax.numpy as jnp
        import numpy as np
        N_NODES = 50000
        N_EDGES = 50000
        D_FEAT = 32
        key = jax.random.key(seed)
        kx, ke = jax.random.split(key)
        x = jax.random.normal(kx, (N_NODES, D_FEAT), dtype=jnp.float32)
        edge_index = jax.random.randint(ke, (2, N_EDGES), 0, N_NODES, dtype=jnp.int64)
        return {'x': x, 'edge_index': edge_index, 'num_nodes': N_NODES}
    _L2_gnn_all = _L2_gnn_setup()
    _L2_gnn_in = {k: v for k, v in _L2_gnn_all.items() if k in ()}
    del _L2_gnn_all

    def _L3_gnn_setup():
        import jax, jax.numpy as jnp
        import numpy as np
        N_NODES = 3125
        N_EDGES = 50000
        HEADS = 8
        CH = 32

        def _gatv2(x, src, dst, Wl, Wr, att, bias):
            H, C = att.shape
            xl = (x @ Wl).reshape(-1, H, C)
            xr = (x @ Wr).reshape(-1, H, C)
            e = jax.nn.leaky_relu(xl[src] + xr[dst], 0.2)
            logits = jnp.einsum('ehc,hc->eh', e, att)
            m = jax.ops.segment_max(logits, dst, num_segments=N_NODES)
            p = jnp.exp(logits - m[dst])
            denom = jax.ops.segment_sum(p, dst, num_segments=N_NODES)
            alpha = p / denom[dst]
            out = jax.ops.segment_sum(alpha[:, :, None] * xl[src], dst, num_segments=N_NODES)
            return out.mean(axis=1) + bias

        def _bn(x, gamma, beta):
            mu = x.mean(axis=0)
            var = jnp.mean((x - mu) ** 2, axis=0)
            return (x - mu) * jax.lax.rsqrt(var + 1e-05) * gamma + beta
        key = jax.random.key(seed)
        ks = jax.random.split(key, 32)
        d = {'patch_embs': jax.random.normal(ks[0], (N_NODES, CH), dtype=jnp.float32), 'edge_index': jax.random.randint(ks[1], (2, N_EDGES), 0, N_NODES, dtype=jnp.int64 if jax.config.read('jax_enable_x64') else jnp.int32), 'edge_attr': jax.random.normal(ks[2], (N_EDGES, 4), dtype=jnp.float32)}
        s = 1.0 / np.sqrt(CH)
        for i, k0 in zip((1, 2, 3), (3, 10, 17)):
            d[f'Wl{i}'] = jax.random.normal(ks[k0 + 0], (CH, HEADS * CH), dtype=jnp.float32) * s
            d[f'Wr{i}'] = jax.random.normal(ks[k0 + 1], (CH, HEADS * CH), dtype=jnp.float32) * s
            d[f'att{i}'] = jax.random.normal(ks[k0 + 2], (HEADS, CH), dtype=jnp.float32) * s
            d[f'b{i}'] = jnp.zeros((CH,), dtype=jnp.float32)
            d[f'g{i}'] = jnp.ones((CH,), dtype=jnp.float32)
            d[f'be{i}'] = jnp.zeros((CH,), dtype=jnp.float32)
        return d
    _L3_gnn_all = _L3_gnn_setup()
    _L3_gnn_in = {k: v for k, v in _L3_gnn_all.items() if k in ('Wl1', 'Wr1', 'att1', 'b1', 'g1', 'be1', 'Wl2', 'Wr2', 'att2', 'b2', 'g2', 'be2', 'Wl3', 'Wr3', 'att3', 'b3', 'g3', 'be3')}
    del _L3_gnn_all
    return {'x': x, 'src': src, 'dst': dst, 'edge_attr_16': edge_attr_16, 'edge_attr_4': edge_attr_4, 'L0_gnn_W': _L0_gnn_in['W'], 'L0_gnn_b': _L0_gnn_in['b'], 'L1_gnn_kernel': _L1_gnn_in['kernel'], 'L1_gnn_bias': _L1_gnn_in['bias'], 'L3_gnn_Wl1': _L3_gnn_in['Wl1'], 'L3_gnn_Wr1': _L3_gnn_in['Wr1'], 'L3_gnn_att1': _L3_gnn_in['att1'], 'L3_gnn_b1': _L3_gnn_in['b1'], 'L3_gnn_g1': _L3_gnn_in['g1'], 'L3_gnn_be1': _L3_gnn_in['be1'], 'L3_gnn_Wl2': _L3_gnn_in['Wl2'], 'L3_gnn_Wr2': _L3_gnn_in['Wr2'], 'L3_gnn_att2': _L3_gnn_in['att2'], 'L3_gnn_b2': _L3_gnn_in['b2'], 'L3_gnn_g2': _L3_gnn_in['g2'], 'L3_gnn_be2': _L3_gnn_in['be2'], 'L3_gnn_Wl3': _L3_gnn_in['Wl3'], 'L3_gnn_Wr3': _L3_gnn_in['Wr3'], 'L3_gnn_att3': _L3_gnn_in['att3'], 'L3_gnn_b3': _L3_gnn_in['b3'], 'L3_gnn_g3': _L3_gnn_in['g3'], 'L3_gnn_be3': _L3_gnn_in['be3']}

def reference(x, src, dst, edge_attr_16, edge_attr_4, L0_gnn_W, L0_gnn_b, L1_gnn_kernel, L1_gnn_bias, L3_gnn_Wl1, L3_gnn_Wr1, L3_gnn_att1, L3_gnn_b1, L3_gnn_g1, L3_gnn_be1, L3_gnn_Wl2, L3_gnn_Wr2, L3_gnn_att2, L3_gnn_b2, L3_gnn_g2, L3_gnn_be2, L3_gnn_Wl3, L3_gnn_Wr3, L3_gnn_att3, L3_gnn_b3, L3_gnn_g3, L3_gnn_be3):
    import jax
    import jax.numpy as jnp

    def _L0_gnn_ref(x, W, b, src, dst):
        import jax, jax.numpy as jnp
        import numpy as np
        N_NODES = 3125
        N_EDGES = 200000
        D = 32
        ones = jnp.ones_like(src, dtype=x.dtype)
        out_deg = jax.ops.segment_sum(ones, src, num_segments=N_NODES)
        in_deg = jax.ops.segment_sum(ones, dst, num_segments=N_NODES)
        out_norm = jax.lax.rsqrt(jnp.maximum(out_deg, 1.0))
        in_norm = jax.lax.rsqrt(jnp.maximum(in_deg, 1.0))
        h = x * out_norm[:, None]
        msgs = h[src]
        agg = jax.ops.segment_sum(msgs, dst, num_segments=N_NODES)
        out = agg * in_norm[:, None] @ W + b
        return out

    def _L1_gnn_ref(atom_features, bond_features, pair_indices, kernel, bias):
        import jax, jax.numpy as jnp
        import numpy as np
        N_ATOMS = 3125
        N_EDGES = 12500
        ATOM_DIM = 32
        BOND_DIM = 16
        n_atoms, d = atom_features.shape
        e = bond_features.shape[0]
        edge_mats = (bond_features @ kernel + bias).reshape(e, d, d)
        neighbors = atom_features[pair_indices[:, 1]]
        transformed = jnp.einsum('eij,ej->ei', edge_mats, neighbors)
        return jax.ops.segment_sum(transformed, pair_indices[:, 0], num_segments=n_atoms)

    def _L2_gnn_ref(x, edge_index, num_nodes):
        import jax, jax.numpy as jnp
        import numpy as np
        N_NODES = 50000
        N_EDGES = 50000
        D_FEAT = 32
        src = edge_index[0]
        dst = edge_index[1]
        msgs = x[src]
        out = jax.ops.segment_sum(msgs, dst, num_segments=num_nodes)
        return out

    def _L3_gnn_ref(patch_embs, edge_index, edge_attr, Wl1, Wr1, att1, b1, g1, be1, Wl2, Wr2, att2, b2, g2, be2, Wl3, Wr3, att3, b3, g3, be3):
        import jax, jax.numpy as jnp
        import numpy as np
        N_NODES = 3125
        N_EDGES = 50000
        HEADS = 8
        CH = 32

        def _gatv2(x, src, dst, Wl, Wr, att, bias):
            H, C = att.shape
            xl = (x @ Wl).reshape(-1, H, C)
            xr = (x @ Wr).reshape(-1, H, C)
            e = jax.nn.leaky_relu(xl[src] + xr[dst], 0.2)
            logits = jnp.einsum('ehc,hc->eh', e, att)
            m = jax.ops.segment_max(logits, dst, num_segments=N_NODES)
            p = jnp.exp(logits - m[dst])
            denom = jax.ops.segment_sum(p, dst, num_segments=N_NODES)
            alpha = p / denom[dst]
            out = jax.ops.segment_sum(alpha[:, :, None] * xl[src], dst, num_segments=N_NODES)
            return out.mean(axis=1) + bias

        def _bn(x, gamma, beta):
            mu = x.mean(axis=0)
            var = jnp.mean((x - mu) ** 2, axis=0)
            return (x - mu) * jax.lax.rsqrt(var + 1e-05) * gamma + beta
        loop = jnp.arange(N_NODES, dtype=edge_index.dtype)
        src = jnp.concatenate([edge_index[0], loop])
        dst = jnp.concatenate([edge_index[1], loop])
        x = patch_embs
        x = _bn(jax.nn.leaky_relu(_gatv2(x, src, dst, Wl1, Wr1, att1, b1), 0.01) + x, g1, be1)
        x = _bn(jax.nn.leaky_relu(_gatv2(x, src, dst, Wl2, Wr2, att2, b2), 0.01) + x, g2, be2)
        x = _bn(_gatv2(x, src, dst, Wl3, Wr3, att3, b3) + x, g3, be3)
        return x
    edge_index = jnp.stack([src, dst])
    edge_index_t = jnp.stack([src, dst], axis=1)
    h = jnp.maximum(_layernorm(x, axis=-1), 0.0)
    x = x + _L0_gnn_ref(h, L0_gnn_W, L0_gnn_b, src, dst)
    h = jnp.maximum(_layernorm(x, axis=-1), 0.0)
    x = x + _L1_gnn_ref(h, edge_attr_16, edge_index_t, L1_gnn_kernel, L1_gnn_bias)
    h = jnp.maximum(_layernorm(x, axis=-1), 0.0)
    x = x + _L2_gnn_ref(h, edge_index, 3125)
    h = jnp.maximum(_layernorm(x, axis=-1), 0.0)
    x = x + _L3_gnn_ref(h, edge_index, edge_attr_4, L3_gnn_Wl1, L3_gnn_Wr1, L3_gnn_att1, L3_gnn_b1, L3_gnn_g1, L3_gnn_be1, L3_gnn_Wl2, L3_gnn_Wr2, L3_gnn_att2, L3_gnn_b2, L3_gnn_g2, L3_gnn_be2, L3_gnn_Wl3, L3_gnn_Wr3, L3_gnn_att3, L3_gnn_b3, L3_gnn_g3, L3_gnn_be3)
    return x

_drawn_inputs = setup_inputs


def setup_inputs(seed=0):
    import zlib

    import numpy as np

    out = dict(_drawn_inputs(seed))
    spreads = {'L0_gnn_b': (0.0, 0.1),
     'L1_gnn_bias': (0.0, 0.1),
     'L3_gnn_b1': (0.0, 0.8),
     'L3_gnn_g1': (1.0, 0.6),
     'L3_gnn_be1': (0.0, 0.8),
     'L3_gnn_b2': (0.0, 2.0),
     'L3_gnn_g2': (1.0, 0.6),
     'L3_gnn_be2': (0.0, 2.0),
     'L3_gnn_b3': (0.0, 2.0),
     'L3_gnn_g3': (1.0, 0.6),
     'L3_gnn_be3': (0.0, 2.0)}
    factors = {'L3_gnn_Wl1': 3.796,
     'L3_gnn_Wr1': 8.0,
     'L3_gnn_att1': 8.0,
     'L3_gnn_Wl2': 7.682,
     'L3_gnn_Wr2': 8.0,
     'L3_gnn_att2': 8.0,
     'L3_gnn_Wl3': 6.117,
     'L3_gnn_Wr3': 23.747,
     'L3_gnn_att3': 8.0}
    for name, (base, spread) in spreads.items():
        noise = np.random.default_rng([zlib.crc32(name.encode()), seed]).standard_normal(out[name].shape)
        drawn = base * np.exp(spread * noise) if base else spread * noise
        out[name] = jnp.asarray(drawn.astype(out[name].dtype))
    for name, factor in factors.items():
        out[name] = (out[name] * factor).astype(out[name].dtype)
    return out
```

```python
from contextlib import ExitStack

import numpy as np
import concourse.bass as bass
from concourse import mybir

F32 = mybir.dt.float32
BF16 = mybir.dt.bfloat16
I32 = mybir.dt.int32
ALU = mybir.AluOpType
ACT = mybir.ActivationFunctionType
AX_X = mybir.AxisListType.X

P = 128
NODES = 3125
EDGES = 100000
D = 32
HEADS = 8
EA = 16
LAYERS = 3
NP5 = 125
NT5 = NODES // NP5
EC = EDGES // NP5
CHUNKS = 16
TILES = 816
TPC = TILES // CHUNKS
CLEN = TPC * P
SLOTS = 832
FIELDS, FEA, FREAL = 20, 2, 18
DFIELDS, DREAL = 4, 2
FKEY, FOTHER = 0, 1
NF = EA + 1
LAG = 3
HALF = 8
WIN = NODES + P
NTAB = 26 * P
GC = 4
SCAT = 16
SELF_CALLS = 35
NHI = 26
BIG = 1.0e30
EPS = 1e-5


class Count:

    def __init__(self, sem):
        self.sem, self.n = sem, 0

    def by(self, instruction, step=1):
        instruction.then_inc(self.sem, step)
        self.n += step
        return self.n


def build(nc, a, out, stop=None):
    top = ExitStack()

    def sem(name):
        return top.enter_context(nc.semaphore(name))

    def sb(stack, name, shape, dt=F32):
        return stack.enter_context(nc.sbuf_tensor(name, shape, dt))

    def ps(stack, name, shape, dt=F32):
        return stack.enter_context(nc.psum_tensor(name, shape, dt))

    def scratch(name, shape, dt=F32):
        return nc.dram_tensor(name, shape, dt, kind="Internal").ap()

    recd_dram = scratch("records_by_destination", [P * SLOTS, DFIELDS])
    recs_dram = scratch("records_by_source", [P * SLOTS, FIELDS])
    htab = scratch("node_table", [NTAB, D])
    degtab = scratch("degrees", [2, NHI * P])
    dst_rows = scratch("dst_rows", [896, P])
    loc_rows = scratch("loc_rows", [896, P])
    xs_dram = scratch("gathered", [P, TILES * D])

    with top:
        ident = sb(top, "ident", [P, P])
        iota = sb(top, "iota", [P, P])
        lanes = sb(top, "lanes", [P, 1])
        ones = sb(top, "ones", [P, P])
        x_sb = sb(top, "x_sb", [NP5, NT5, D])
        stat = sb(top, "stat", [NP5, 2, NT5])
        tmp = sb(top, "tmp", [NP5, NT5, D])
        h_sb = sb(top, "h_sb", [NP5, NT5, D])
        onorm = sb(top, "onorm", [NP5, NT5])
        inorm = sb(top, "inorm", [NP5, NT5])
        src_all = sb(top, "src_all", [P, SLOTS])
        loc_full = sb(top, "loc_full", [P, TILES])
        base_i = sb(top, "base_i", [1, TILES], I32)

        loads = Count(sem("constant_loads"))
        chain = Count(sem("vector_chain"))
        act_done = Count(sem("scalar_step"))
        pe_done = Count(sem("tensor_step"))
        pool_turns = sem("pool_turns")
        stored = Count(sem("table_stored"))

        def link(eng, instruction):
            eng.wait_ge(chain.sem, chain.by(instruction))

        def layer_norm(dve, act_steps, scale=None):
            link(dve, dve.reduce_sum(stat[:, 0, :], x_sb[:, :, :], AX_X))
            link(dve, dve.tensor_scalar(stat[:, 0, :], stat[:, 0, :], 1.0 / D, None, ALU.mult))
            link(dve, dve.tensor_tensor(h_sb[:, :, :], x_sb[:, :, :],
                                        stat[:, 0, :].unsqueeze(2).to_broadcast([NP5, NT5, D]), ALU.subtract))
            link(dve, dve.tensor_tensor(tmp[:, :, :], h_sb[:, :, :], h_sb[:, :, :], ALU.mult))
            link(dve, dve.reduce_sum(stat[:, 1, :], tmp[:, :, :], AX_X))
            link(dve, dve.tensor_scalar(stat[:, 1, :], stat[:, 1, :], 1.0 / D, EPS, ALU.mult, ALU.add))
            ready = chain.n
            act_steps.append(ready)
            act_done.n += 1
            dve.wait_ge(act_done.sem, act_done.n)
            link(dve, dve.reciprocal(stat[:, 1, :], stat[:, 1, :]))
            link(dve, dve.tensor_tensor(h_sb[:, :, :], h_sb[:, :, :],
                                        stat[:, 1, :].unsqueeze(2).to_broadcast([NP5, NT5, D]), ALU.mult))
            link(dve, dve.tensor_scalar(h_sb[:, :, :], h_sb[:, :, :], 0.0, None, ALU.max))
            if scale is not None:
                link(dve, dve.tensor_tensor(h_sb[:, :, :], h_sb[:, :, :],
                                            scale[:, :].unsqueeze(2).to_broadcast([NP5, NT5, D]), ALU.mult))

        def root_steps(act, act_steps):
            for ready in act_steps:
                act.wait_ge(chain.sem, ready)
                act.activation(stat[:, 1, :], stat[:, 1, :], ACT.Sqrt).then_inc(act_done.sem, 1)

        with ExitStack() as st:
            ends_n = sb(st, "ends_n", [NP5, 2, EC], I32)
            work_i = sb(st, "work_i", [NP5, EC], I32)
            lo_b = sb(st, "lo_b", [NP5, 2, EC], BF16)
            hi_b = sb(st, "hi_b", [NP5, 2, EC], BF16)
            iota_b = sb(st, "iota_b", [P, P], BF16)
            ident_b = sb(st, "ident_b", [P, P], BF16)
            tri = sb(st, "tri", [P, P])
            earlier = sb(st, "earlier", [P, GC * NP5])
            ea_in = sb(st, "ea_in", [NP5, 2, SCAT * EA])
            recd_in = sb(st, "recd_in", [NP5, 2, SCAT, DFIELDS])
            recs_in = sb(st, "recs_in", [NP5, 2, SCAT, FIELDS])
            one_lo = sb(st, "one_lo", [NP5, 2, 2, SCAT, P], BF16)
            one_hi = sb(st, "one_hi", [NP5, 2, 2, SCAT, NHI], BF16)
            zero_b = sb(st, "zero_b", [P, P], BF16)
            cnt = sb(st, "cnt", [P, 2, NHI])
            offs = sb(st, "offs", [P, 2, NHI])
            node_f = sb(st, "node_f", [P, SELF_CALLS])
            self_pos = sb(st, "self_pos", [P, 2, SELF_CALLS])
            self_row = sb(st, "self_row", [P, 2, SELF_CALLS], I32)
            selfd_rec = sb(st, "selfd_rec", [P, SELF_CALLS, DFIELDS])
            selfs_rec = sb(st, "selfs_rec", [P, SELF_CALLS, FIELDS])
            zpad = sb(st, "zpad", [P, D])
            lo_turned = sb(st, "lo_turned", [P, 2, 2, GC * NP5])
            before = sb(st, "before", [P, 2, NHI])
            same_key = sb(st, "same_key", [NP5, 2, 2, GC, GC * NP5], BF16)
            picked = sb(st, "picked", [NP5, 2, 2, GC, NHI])
            rank = sb(st, "rank", [NP5, 2, 2, SCAT])
            place = sb(st, "place", [NP5, 2, 2, SCAT])
            key_in = sb(st, "key_in", [NP5, 2, 2, SCAT])
            row_in = sb(st, "row_in", [NP5, 2, 2, SCAT], I32)

            consts_ready = sem("consts_ready")
            ea_loaded = [sem(f"ea_loaded{h}") for h in range(2)]
            recs_ready = sem("recs_ready")
            recs_free = sem("recs_free")
            ea_used = sem("ea_used")
            scattered = [sem(f"scattered{h}") for h in range(2)]
            onehots_ready = sem("onehots_ready")
            onehots_used = sem("onehots_used")
            self_scattered = sem("self_scattered")
            degrees_ready = sem("degrees_ready")
            degs_loaded = sem("degs_loaded")
            col_turned = sem("col_turned")
            col_copied = sem("col_copied")
            col_looked = sem("col_looked")
            col_counted = sem("col_counted")
            col_carried = sem("col_carried")
            col_ranked = sem("col_ranked")
            row_chain = sem("row_chain")
            steps = EC // (2 * SCAT)
            ROW_STEPS = 11

            def row_ops(dve, shape_of, pos_f, out_row):
                p_i, t_i, c_i = shape_of("p_i", I32), shape_of("t_i", I32), shape_of("c_i", I32)
                t_f, c_f, s_f = shape_of("t_f", F32), shape_of("c_f", F32), shape_of("s_f", F32)
                up = 1286
                return [
                    lambda: dve.tensor_copy(p_i, pos_f),
                    lambda: dve.tensor_scalar(t_i, p_i, 7, None, ALU.arith_shift_right),
                    lambda: dve.tensor_copy(t_f, t_i),
                    lambda: dve.tensor_scalar(c_i, t_f, float(up), None, ALU.mult),
                    lambda: dve.tensor_scalar(c_i, c_i, 16, None, ALU.arith_shift_right),
                    lambda: dve.tensor_scalar(c_f, c_i, float(CHUNKS - 1), float(-(CHUNKS * TPC - 1)), ALU.min, ALU.mult),
                    lambda: dve.scalar_tensor_tensor(s_f, t_f, float(CHUNKS), c_f, ALU.mult, ALU.add),
                    lambda: dve.tensor_scalar(p_i, p_i, P - 1, None, ALU.bitwise_and),
                    lambda: dve.tensor_copy(t_f, p_i),
                    lambda: dve.scalar_tensor_tensor(out_row, t_f, float(SLOTS), s_f, ALU.mult, ALU.add),
                ]

            def work_tiles(name, parts, shape):
                made = {}

                def get(which, dt):
                    if which not in made:
                        made[which] = sb(st, f"{name}_{which}", [parts, *shape], dt)
                    return made[which][tuple(slice(None) for _ in range(len(shape) + 1))]
                return get

            loop_work = work_tiles("places", NP5, [2, SCAT])
            self_work = work_tiles("selfs", P, [2, SELF_CALLS])

            def one_hots(dve, h, col):
                for k in range(2):
                    dve.tensor_tensor(
                        one_lo[:, h, k, :, :],
                        iota_b[0:NP5, :].unsqueeze(1).to_broadcast([NP5, SCAT, P]),
                        lo_b[:, k, bass.ds(col, SCAT)].unsqueeze(2).to_broadcast([NP5, SCAT, P]),
                        ALU.is_equal)
                    last = dve.tensor_tensor(
                        one_hi[:, h, k, :, :],
                        iota_b[0:NP5, 0:NHI].unsqueeze(1).to_broadcast([NP5, SCAT, NHI]),
                        hi_b[:, k, bass.ds(col, SCAT)].unsqueeze(2).to_broadcast([NP5, SCAT, NHI]),
                        ALU.is_equal)
                return last

            with ExitStack() as inner, nc.Block() as block:
                hist = ps(inner, "hist", [P, 2, 512])
                hsum = ps(inner, "hsum", [P, 2, 2, NHI])

                @block.sync
                def _(sp):
                    for dst_ap, src_ap in (
                            (ident[:, :], a["c_ident"]), (iota[:, :], a["c_iota"]), (lanes[:, :], a["c_lanes"]),
                            (tri[:, :], a["c_tri"]), (earlier[:, :], a["c_earlier"]), (node_f[:, :], a["c_node"]),
                            (ends_n[:, 0, :], a["dst"].rearrange("(p i) -> p i", p=NP5)),
                            (ends_n[:, 1, :], a["src"].rearrange("(p i) -> p i", p=NP5)),
                            (x_sb[:, :, :], a["x"].rearrange("(p t) d -> p t d", p=NP5))):
                        loads.by(sp.dma_start(dst_ap, src_ap), 16)

                @block.vector
                def _(dve):
                    link(dve, dve.memset(ones[:, :], 1.0))
                    link(dve, dve.memset(zero_b[:, :], 0.0))
                    link(dve, dve.memset(recd_in[:, :, :, :], 0.0))
                    link(dve, dve.memset(recs_in[:, :, :, :], 0.0))
                    link(dve, dve.memset(recd_in[:, :, :, DREAL:DREAL + 1], 1.0))
                    link(dve, dve.memset(recs_in[:, :, :, FREAL:FREAL + 1], 1.0))
                    link(dve, dve.memset(selfd_rec[:, :, :], 0.0))
                    link(dve, dve.memset(selfs_rec[:, :, :], 0.0))
                    link(dve, dve.memset(zpad[:, :], 0.0))
                    dve.wait_ge(loads.sem, 16 * 9)
                    link(dve, dve.tensor_copy(iota_b[:, :], iota[:, :]))
                    link(dve, dve.tensor_copy(ident_b[:, :], ident[:, :]))
                    for k in range(2):
                        link(dve, dve.tensor_scalar(work_i[:, :], ends_n[:, k, :], P - 1, None, ALU.bitwise_and))
                        link(dve, dve.tensor_copy(lo_b[:, k, :], work_i[:, :]))
                        link(dve, dve.tensor_scalar(work_i[:, :], ends_n[:, k, :], 7, None, ALU.arith_shift_right))
                        link(dve, dve.tensor_copy(hi_b[:, k, :], work_i[:, :]))
                    dve.sem_inc(consts_ready, 1)
                    dve.sem_inc(onehots_used, 2)
                    with dve.Fori(0, steps) as i:
                        for h in range(2):
                            dve.wait_ge(onehots_used, 2 * i + (h + 1))
                            one_hots(dve, h, i * (2 * SCAT) + h * SCAT).then_inc(onehots_ready, 1)
                    dve.wait_ge(pe_done.sem, 1)
                    link(dve, dve.tensor_copy(cnt[:, :, :], hist[:, :, 0:NHI]))
                    dve.sem_inc(degrees_ready, 1)
                    dve.wait_ge(pe_done.sem, 2)
                    link(dve, dve.memset(offs[:, :, :], 0.0))
                    for k in range(2):
                        link(dve, dve.tensor_tensor_scan(offs[:, k, 1:NHI], ones[:, 0:NHI - 1], hsum[:, 1, k, 0:NHI - 1],
                                                         0.0, ALU.mult, ALU.add))
                        link(dve, dve.tensor_scalar(self_pos[:, k, :], node_f[:, :], float(EDGES), None, ALU.add))
                        link(dve, dve.tensor_tensor(offs[:, k, :], offs[:, k, :], hsum[:, 0, k, :], ALU.add))
                        link(dve, dve.tensor_tensor(self_pos[:, k, 0:NHI], offs[:, k, :], node_f[:, 0:NHI], ALU.add))
                    link(dve, dve.tensor_scalar(before[:, :, :], self_pos[:, :, 0:NHI], 1.0, None, ALU.add))
                    for op in row_ops(dve, self_work, self_pos[:, :, :], self_row[:, :, :]):
                        link(dve, op())
                    real = self_work("c_f", F32)[:, 0, :]
                    link(dve, dve.tensor_scalar(real, node_f[:, :], float(NODES), None, ALU.is_lt))
                    for rec in (selfd_rec, selfs_rec):
                        link(dve, dve.tensor_scalar(rec[:, :, FKEY], node_f[:, :], float(NODES), None, ALU.min))
                        link(dve, dve.tensor_tensor(rec[:, :, FOTHER], node_f[:, :], real, ALU.mult))

                @block.tensor
                def _(pe):
                    pe.wait_ge(consts_ready, 1)
                    for k in range(2):
                        pe.matmul(hist[:, k, 0:NHI], zero_b[:, :], zero_b[:, 0:NHI], start=True, stop=False)
                    with pe.Fori(0, steps) as i:
                        for h in range(2):
                            pe.wait_ge(onehots_ready, 2 * i + (h + 1))
                            for k in range(2):
                                for u in range(SCAT):
                                    last = pe.matmul(hist[:, k, 0:NHI], one_lo[:, h, k, u, :], one_hi[:, h, k, u, :],
                                                     start=False, stop=False)
                            last.then_inc(onehots_used, 1)
                    for k in range(2):
                        last = pe.matmul(hist[:, k, 0:NHI], zero_b[:, :], zero_b[:, 0:NHI], start=False, stop=True)
                    pe_done.by(last)
                    pe.wait_ge(degrees_ready, 1)
                    pe.matmul(hsum[:, 0, :, :], tri[:, :], cnt[:, :, :], start=True, stop=True)
                    pe_done.by(pe.matmul(hsum[:, 1, :, :], ones[:, :], cnt[:, :, :], start=True, stop=True))

                @block.scalar
                def _(act):
                    act.wait_ge(degrees_ready, 1)
                    stored.by(act.dma_start(degtab.rearrange("k (h l) -> l k h", l=P), cnt[:, :, :],
                                            allow_slow_non_contiguous=True), 16)
                    stored.by(act.dma_start(htab[NODES:NODES + P, :], zpad[:, :]), 16)
                    stored.by(act.dma_start(htab[NODES + P:NTAB, :], zpad[0:NTAB - NODES - P, :]), 16)
                    act.wait_ge(stored.sem, stored.n)
                    for k, deg in enumerate((inorm, onorm)):
                        act.dma_start(deg[:, :], degtab[k, 0:NODES].rearrange("(p t) -> p t", p=NP5)
                                      ).then_inc(degs_loaded, 16)
                    act.wait_ge(degs_loaded, 32)

            with ExitStack() as inner, nc.Block() as block:
                keys = ps(inner, "keys", [NP5, 2, 2, 512])
                turned = ps(inner, "turned_lo", [P, 2, 2, 512], BF16)
                found = ps(inner, "found", [NP5, 512])
                count = ps(inner, "count", [P, 512])
                TSTEP = 512 // GC
                GPH = SCAT // GC

                def group(i, h, v):
                    return i * (2 * GPH) + (h * GPH + v)

                @block.sync
                def _(sp):
                    ea = a["edge_attr_16"].rearrange("(p i) k -> p i k", p=NP5)
                    with sp.Fori(0, steps) as i:
                        for h in range(2):
                            sp.wait_ge(ea_used, 2 * i + (h + 1))
                            sp.dma_start(ea_in[:, h, :].rearrange("p (i k) -> p i k", k=EA),
                                         ea[:, bass.ds(i * (2 * SCAT) + h * SCAT, SCAT), :]).then_inc(ea_loaded[h], 16)

                @block.vector
                def _(dve):
                    dve.sem_inc(ea_used, 2)
                    dve.sem_inc(recs_free, 2)
                    dve.sem_inc(col_ranked, 2)

                    def prepare(i, h):
                        col = i * (2 * SCAT) + h * SCAT
                        dve.wait_ge(col_counted, (2 * GPH) * i + (GPH * h + GPH))
                        dve.tensor_copy(key_in[:, h, :, :], ends_n[:, :, bass.ds(col, SCAT)])
                        one_hots(dve, h, col).then_inc(onehots_ready, 1)

                    def rank_group(i, h, v):
                        dve.wait_ge(col_turned, group(i, h, v) + 1)
                        for w in range(GC):
                            u = GC * v + w
                            for k in range(2):
                                dve.scalar_tensor_tensor(
                                    same_key[:, v % 2, k, w, 0:NP5 * (w + 1)], keys[:, v % 2, k, 0:NP5 * (w + 1)],
                                    key_in[:, h, k, u:u + 1], earlier[0:NP5, NP5 * (GC - 1 - w):NP5 * GC],
                                    ALU.is_equal, ALU.mult, accum_out=rank[:, h, k, u:u + 1])
                        dve.wait_ge(col_looked, group(i, h, v) + 3)
                        for w in range(GC):
                            u = GC * v + w
                            for k in range(2):
                                at = NHI * (2 * w + k)
                                last = dve.scalar_tensor_tensor(
                                    picked[:, v % 2, k, w, :], found[:, at:at + NHI], 1.0, one_hi[:, h, k, u, :],
                                    ALU.mult, ALU.mult, accum_out=place[:, h, k, u:u + 1])
                        last.then_inc(col_ranked, 1)

                    def finish(i, h):
                        col = i * (2 * SCAT) + h * SCAT
                        dve.wait_ge(recs_free, 2 * i + (h + 1))
                        dve.wait_ge(ea_loaded[h], 16 * i + 16)
                        dve.tensor_copy(recs_in[:, h, :, FEA:FEA + EA],
                                        ea_in[:, h, :].rearrange("p (i k) -> p i k", k=EA)).then_inc(ea_used, 1)
                        for k, rec in enumerate((recd_in, recs_in)):
                            dve.tensor_copy(rec[:, h, :, FKEY], ends_n[:, k, bass.ds(col, SCAT)])
                            dve.tensor_copy(rec[:, h, :, FOTHER], ends_n[:, 1 - k, bass.ds(col, SCAT)])
                        dve.wait_ge(col_ranked, group(i, h, GPH - 1) + 3)
                        ops = [lambda: dve.tensor_tensor(place[:, h, :, :], place[:, h, :, :], rank[:, h, :, :], ALU.add)]
                        ops += row_ops(dve, loop_work, place[:, h, :, :], row_in[:, h, :, :])
                        for n, op in enumerate(ops):
                            op().then_inc(row_chain, 1)
                            dve.wait_ge(row_chain, (2 * ROW_STEPS) * i + (ROW_STEPS * h + n + 1))
                        dve.sem_inc(recs_ready, 1)

                    def half(i, h, more):
                        for v in range(GPH):
                            if v == GPH // 2 and more:
                                prepare(i + h, 1 - h)
                            rank_group(i, h, v)
                        finish(i, h)

                    prepare(0, 0)
                    with dve.Fori(0, steps - 1) as i:
                        half(i, 0, True)
                        half(i, 1, True)
                    half(steps - 1, 0, True)
                    half(steps - 1, 1, False)

                @block.tensor
                def _(pe):
                    pe.sem_inc(col_counted, 2 * GPH)
                    pe.sem_inc(col_looked, 2)

                    def turn(i, h, v):
                        pe.wait_ge(col_ranked, group(i, h, v) + 1)
                        for w in range(GC):
                            edges = slice(NP5 * w, NP5 * w + NP5)
                            for k in range(2):
                                u = GC * v + w
                                pe.matmul(keys[:, v % 2, k, edges], key_in[:, h, k, u:u + 1].to_broadcast([NP5, NP5]),
                                          ident[0:NP5, 0:NP5], start=True, stop=True)
                                last = pe.transpose(turned[:, v % 2, k, TSTEP * w:TSTEP * w + NP5],
                                                    one_lo[:, h, k, u, :], ident_b[0:NP5, 0:NP5])
                        last.then_inc(col_turned, 1)

                    def look_and_count(i, h, v):
                        g = group(i, h, v)
                        pe.wait_ge(col_copied, g + 1)
                        pe.wait_ge(col_carried, g + 1)
                        pe.wait_ge(col_ranked, g + 2)
                        for w in range(GC):
                            for k in range(2):
                                at = NHI * (2 * w + k)
                                last = pe.matmul(found[:, at:at + NHI], lo_turned[:, v % 2, k, NP5 * w:NP5 * w + NP5],
                                                 before[:, k, :], start=True, stop=True)
                        last.then_inc(col_looked, 1)
                        pe.matmul(count[:, 0:2 * NHI], ident[:, :], before[:, :, :], start=True, stop=False)
                        for w in range(GC):
                            for k in range(2):
                                last = pe.matmul(count[:, NHI * k:NHI * k + NHI], one_lo[:, h, k, GC * v + w, :],
                                                 one_hi[:, h, k, GC * v + w, :], start=False,
                                                 stop=(k == 1 and w == GC - 1))
                        last.then_inc(col_counted, 1)

                    with pe.Fori(0, steps) as i:
                        for h in range(2):
                            pe.wait_ge(onehots_ready, 2 * i + (h + 1 + 2 * steps))
                            turn(i, h, 0)
                            for v in range(GPH):
                                if v + 1 < GPH:
                                    turn(i, h, v + 1)
                                look_and_count(i, h, v)

                @block.scalar
                def _(act):
                    def copy_turned(i, h, v):
                        g = group(i, h, v)
                        act.wait_ge(col_turned, g + 1)
                        act.wait_ge(col_looked, g + 1)
                        act.activation(lo_turned[:, v % 2, :, :].rearrange("p k (w n) -> p k w n", n=NP5),
                                       turned[:, v % 2, :, :].rearrange("p k (w n) -> p k w n", n=TSTEP)[:, :, :, 0:NP5],
                                       ACT.Copy).then_inc(col_copied, 1)

                    act.sem_inc(col_carried, 1)
                    with act.Fori(0, steps) as i:
                        for h in range(2):
                            copy_turned(i, h, 0)
                            for v in range(GPH):
                                if v + 1 < GPH:
                                    copy_turned(i, h, v + 1)
                                act.wait_ge(col_counted, group(i, h, v) + (2 * GPH + 1))
                                act.activation(before[:, :, :], count[:, 0:2 * NHI].rearrange("p (k n) -> p k n", k=2),
                                               ACT.Copy).then_inc(col_carried, 1)

                @block.gpsimd
                def _(pool):
                    for u in range(SELF_CALLS):
                        for k, (table, rec) in enumerate(((recd_dram, selfd_rec), (recs_dram, selfs_rec))):
                            pool.indirect_dma_start(
                                out=table, out_offset=bass.IndirectOffsetOnAxis(ap=self_row[:, k, u:u + 1], axis=0),
                                in_=rec[:, u, :], in_offset=None).then_inc(self_scattered, 16)

                    def scatter(h, half_number, free_other):
                        pool.wait_ge(recs_ready, half_number)
                        pool.sem_inc(pool_turns, 1)
                        for u in range(SCAT):
                            if u == SCAT // 2 and free_other is not None:
                                pool.wait_ge(scattered[1 - h], free_other)
                                pool.sem_inc(recs_free, 1)
                            for k, (table, rec) in enumerate(((recd_dram, recd_in), (recs_dram, recs_in))):
                                pool.indirect_dma_start(
                                    out=table, out_offset=bass.IndirectOffsetOnAxis(ap=row_in[:, h, k, u:u + 1], axis=0),
                                    in_=rec[:, h, u, :], in_offset=None).then_inc(scattered[h], 16)

                    per = 2 * 16 * SCAT
                    scatter(0, 1, None)
                    with pool.Fori(0, steps - 1) as i:
                        scatter(1, 2 * i + 2, per * i + per)
                        scatter(0, 2 * i + 3, per * i + per)
                    scatter(1, 2 * steps, per * steps)
                    pool.wait_ge(scattered[1], per * steps)
                    pool.wait_ge(self_scattered, 2 * 16 * SELF_CALLS)

        rec_stack = top.enter_context(ExitStack())
        fac = sb(rec_stack, "fac", [P, TILES, NF])
        local = sb(rec_stack, "local", [P, TILES])
        dst_all = sb(rec_stack, "dst_all", [P, TILES])
        src_local = sb(rec_stack, "src_local", [P, TILES])
        src_base = sb(rec_stack, "src_base", [1, TILES], I32)
        with ExitStack() as st:
            CUT = 4
            part = TILES // CUT
            rec = sb(st, "rec", [P, 2, part, FIELDS])
            recd = sb(st, "recd", [P, TILES, DFIELDS])
            key_all = sb(st, "key_all", [P, 2, 896])
            loc_all = sb(st, "loc_all", [P, 896])
            rows_sb = sb(st, "rows_sb", [P, 14, P])
            bcast = ps(st, "bcast", [P, 2, 512])
            turned = ps(st, "turned", [P, 4, 512])
            recd_loaded = sem("recd_loaded")
            rec_loaded = [sem(f"rec_loaded{h}") for h in range(2)]
            rec_used = sem("rec_used")
            keys_ready = sem("keys_ready")
            bases_done = sem("bases_done")
            bases_used = sem("bases_used")
            loc_ready = sem("loc_ready")
            turned_done = sem("turned_done")
            turned_used = sem("turned_used")
            rows_stored = sem("rows_stored")
            with nc.Block() as block:

                @block.sync
                def _(sp):
                    sp.dma_start(recd[:, :, :], recd_dram.rearrange("(p s) f -> p s f", s=SLOTS)[:, 0:TILES, :]
                                 ).then_inc(recd_loaded, 16)
                    rt = recs_dram.rearrange("(p s) f -> p s f", s=SLOTS)
                    for c in range(CUT):
                        if c >= 2:
                            sp.wait_ge(rec_used, c - 1)
                        sp.dma_start(rec[:, c % 2, :, :], rt[:, c * part:(c + 1) * part, :]
                                     ).then_inc(rec_loaded[c % 2], 16)
                    for k, table in enumerate((dst_rows, loc_rows)):
                        sp.wait_ge(turned_used, 7 * (k + 1))
                        sp.dma_start(table.rearrange("(b o) e -> o b e", o=P), rows_sb[:, 7 * k:7 * k + 7, :]
                                     ).then_inc(rows_stored, 16)
                    sp.wait_ge(rows_stored, 32)

                @block.vector
                def _(dve):
                    link(dve, dve.memset(src_all[:, TILES:SLOTS], 0.0))
                    link(dve, dve.memset(key_all[:, :, TILES:896], float(NODES)))
                    link(dve, dve.memset(loc_all[:, TILES:896], 0.0))
                    dve.wait_ge(recd_loaded, 16)
                    dve.tensor_copy(src_all[:, 0:TILES], recd[:, :, FOTHER])
                    link(dve, dve.tensor_copy(key_all[:, 0, 0:TILES], recd[:, :, FKEY]))
                    for c in range(CUT):
                        dve.wait_ge(rec_loaded[c % 2], 16 * (c // 2 + 1))
                        cols = slice(c * part, (c + 1) * part)
                        dve.tensor_copy(dst_all[:, cols], rec[:, c % 2, :, FOTHER])
                        dve.tensor_copy(key_all[:, 1, cols], rec[:, c % 2, :, FKEY])
                        link(dve, dve.tensor_copy(fac[:, cols, :], rec[:, c % 2, :, FEA:FEA + NF]))
                        dve.sem_inc(rec_used, 1)
                    link(dve, dve.tensor_copy(base_i[:, :], key_all[0:1, 0, 0:TILES]))
                    link(dve, dve.tensor_copy(src_base[:, :], key_all[0:1, 1, 0:TILES]))
                    dve.sem_inc(keys_ready, 1)
                    for lst, loc in enumerate((loc_all, src_local)):
                        dve.wait_ge(bases_done, lst + 1)
                        for k in range(2):
                            cols = slice(408 * k, 408 * k + 408)
                            link(dve, dve.tensor_tensor(loc[:, cols], key_all[:, lst, cols], bcast[:, k, 0:408],
                                                        ALU.subtract))
                        dve.sem_inc(bases_used, 1)
                    link(dve, dve.tensor_copy(loc_full[:, :], loc_all[:, 0:TILES]))
                    link(dve, dve.scalar_tensor_tensor(local[:, :], loc_all[:, 0:TILES], 1.0, recd[:, :, DREAL],
                                                       ALU.add, ALU.mult))
                    link(dve, dve.tensor_scalar(local[:, :], local[:, :], -1.0, None, ALU.add))
                    for deg in (onorm, inorm):
                        link(dve, dve.tensor_scalar(deg[:, :], deg[:, :], 1.0, None, ALU.max))
                    dve.sem_inc(keys_ready, 1)
                    dve.wait_ge(act_done.sem, 2)
                    for deg in (onorm, inorm):
                        link(dve, dve.reciprocal(deg[:, :], deg[:, :]))

                @block.tensor
                def _(pe):
                    pe.wait_ge(keys_ready, 1)
                    for lst in range(2):
                        if lst:
                            pe.wait_ge(bases_used, 1)
                        for k in range(2):
                            last = pe.matmul(bcast[:, k, 0:408], ones[0:1, :], key_all[0:1, lst, 408 * k:408 * k + 408],
                                             start=True, stop=True)
                        last.then_inc(bases_done, 1)
                    for b in range(14):
                        if b == 7:
                            pe.wait_ge(bases_used, 1)
                        if b >= 4:
                            pe.wait_ge(turned_used, b - 3)
                        cols = slice(P * (b % 7), P * (b % 7) + P)
                        pe.transpose(turned[:, b % 4, 0:P], key_all[:, 0, cols] if b < 7 else loc_all[:, cols], ident[:, :]
                                     ).then_inc(turned_done, 1)

                @block.scalar
                def _(act):
                    for b in range(14):
                        act.wait_ge(turned_done, b + 1)
                        act.activation(rows_sb[:, b, :], turned[:, b % 4, 0:P], ACT.Copy).then_inc(turned_used, 1)
                    act.wait_ge(keys_ready, 2)
                    for deg in (onorm, inorm):
                        act_done.by(act.activation(deg[:, :], deg[:, :], ACT.Sqrt))

        w0 = sb(rec_stack, "w0", [D, D])
        b0 = sb(rec_stack, "b0", [NP5, D])
        k1 = sb(rec_stack, "k1", [D, NF, D])
        k1t = sb(rec_stack, "k1t", [P, 5, D])
        sums = sb(rec_stack, "sums", [P, 4, WIN])
        sums_b = sb(rec_stack, "sums_b", [D, WIN])

        def window_starts(eng, bases, j, h):
            _, starts = nc.values_load_multi_w_load_instructions(
                bases[0:1, bass.ds(j * CHUNKS + h * HALF, HALF)], engines=(eng.engine,), min_val=0, max_val=NODES,
                skip_runtime_bounds_check_because="they are nodes, or NODES for the padding")
            return starts

        def update_block(stage):
            steps = []
            with ExitStack() as st, nc.Block() as block:
                prod = ps(st, f"prod{stage}", [P, 2, 512]) if stage >= 0 else None
                kt_ps = ps(st, f"kt_ps{stage}", [P, 5, D]) if stage < 0 else None
                turned_k = sem(f"turned_k{stage}")
                products = sem(f"products{stage}")
                h_ready = sem(f"h_ready{stage}")
                weights = sem(f"weights{stage}")

                @block.vector
                def _(dve):
                    if stage < 0:
                        dve.wait_ge(turned_k, 1)
                        for q in range(5):
                            rows = P if q < 4 else D
                            link(dve, dve.tensor_copy(k1t[0:rows, q, :], kt_ps[0:rows, q, :]))
                    else:
                        dve.wait_ge(products, 1)
                        for k, (lo, hi) in enumerate(((0, 16), (16, NT5))):
                            got = prod[0:NP5, k, 0:D * (hi - lo)].rearrange("p (t d) -> p t d", d=D)
                            upd = x_sb[:, lo:hi, :]
                            if stage == 0:
                                part = tmp[:, lo:hi, :]
                                link(dve, dve.tensor_tensor(part, got, inorm[:, lo:hi].unsqueeze(2).to_broadcast(
                                    [NP5, hi - lo, D]), ALU.mult))
                                link(dve, dve.tensor_tensor(part, part, b0[:, :].unsqueeze(1).to_broadcast(
                                    [NP5, hi - lo, D]), ALU.add))
                                link(dve, dve.tensor_tensor(upd, upd, part, ALU.add))
                            else:
                                link(dve, dve.tensor_tensor(upd, upd, got, ALU.add))
                    layer_norm(dve, steps, scale=onorm if stage < 0 else None)
                    dve.sem_inc(h_ready, 1)

                @block.scalar
                def _(act):
                    root_steps(act, steps)

                @block.tensor
                def _(pe):
                    if stage < 0:
                        pe.wait_ge(weights, 64)
                        for q in range(5):
                            n = 4 if q < 4 else 1
                            last = pe.transpose(kt_ps[0:n * D, q, :],
                                                k1[:, 4 * q:4 * q + n, :].rearrange("i k j -> i (k j)"),
                                                ident[0:D, 0:D])
                        last.then_inc(turned_k, 1)
                    else:
                        for t in range(NT5):
                            got = prod[0:NP5, t // 16, D * (t % 16):D * (t % 16) + D]
                            cols = slice(t, t + NT5 * (NP5 - 1) + 1, NT5)
                            if stage == 0:
                                last = pe.matmul(got, sums[0:D, 0, cols], w0[:, :], start=True, stop=True)
                            elif stage == 1:
                                for q in range(4):
                                    pe.matmul(got, sums[:, q, cols], k1t[:, q, :], start=(q == 0), stop=False)
                                last = pe.matmul(got, sums_b[:, cols], k1t[0:D, 4, :], start=False, stop=True)
                            else:
                                last = pe.matmul(got, sums[0:D, 0, cols], ident[0:D, 0:D], start=True, stop=True)
                        last.then_inc(products, 1)

                @block.sync
                def _(sp):
                    if stage < 0:
                        sp.dma_start(w0[:, :], a["L0_gnn_W"]).then_inc(weights, 16)
                        sp.dma_start(b0[:, :], a["L0_gnn_b"].unsqueeze(0).to_broadcast([NP5, D])).then_inc(weights, 16)
                        sp.dma_start(k1[:, 0:EA, :], a["L1_gnn_kernel"].rearrange("k (i j) -> i k j", j=D)
                                     ).then_inc(weights, 16)
                        sp.dma_start(k1[:, EA, :], a["L1_gnn_bias"].rearrange("(i j) -> i j", j=D)
                                     ).then_inc(weights, 16)
                        sp.wait_ge(weights, 64)
                    sp.wait_ge(h_ready, 1)
                    stored.by(sp.dma_start(htab[0:NODES, :].rearrange("(p t) d -> p t d", p=NP5), h_sb[:, :, :]), 16)
                    sp.wait_ge(stored.sem, stored.n)

        def aggregate(stage):
            wide = stage == 1
            rows_of, window_of, base_of = (dst_all, src_local, src_base) if wide else (src_all, local, base_i)
            with ExitStack() as st, nc.Block() as block:
                xs = sb(st, f"xs{stage}", [P, 2, HALF * D])
                idx = sb(st, f"idx{stage}", [P, 2, HALF], I32)
                hot = sb(st, f"hot{stage}", [P, 2, HALF, P])
                W = sb(st, f"W{stage}", [P, 4, NF * D]) if wide else None
                acc = ps(st, f"acc{stage}", [P, 2, 512])
                acc_b = ps(st, f"acc_b{stage}", [D, 2, 512]) if wide else None
                idx_ready = sem(f"idx_ready{stage}")
                gathered = [sem(f"gathered{stage}{h}") for h in range(2)]
                hot_ready = sem(f"hot_ready{stage}")
                w_ready = sem(f"w_ready{stage}")
                part_ready = sem(f"part_ready{stage}")
                part_added = sem(f"part_added{stage}")

                @block.scalar
                def _(act):
                    with act.Fori(0, TPC) as j:
                        for h in range(2):
                            act.wait_ge(part_ready, 16 * j + (8 * h + 8))
                            act.activation(idx[:, h, :], rows_of[:, bass.ds(j * CHUNKS + h * HALF, HALF)], ACT.Copy
                                           ).then_inc(idx_ready, 1)

                @block.gpsimd
                def _(pool):
                    with pool.Fori(0, TPC) as j:
                        for h in range(2):
                            pool.wait_ge(idx_ready, 2 * j + (h + 1))
                            pool.sem_inc(pool_turns, 1)
                            for u in range(HALF):
                                pool.indirect_dma_start(
                                    out=xs[:, h, D * u:D * u + D], out_offset=None, in_=htab,
                                    in_offset=bass.IndirectOffsetOnAxis(ap=idx[:, h, u:u + 1], axis=0)
                                ).then_inc(gathered[h], 16)

                @block.tensor
                def _(pe):
                    pe.sem_inc(part_ready, 16)
                    with pe.Fori(0, TPC) as j:
                        for h in range(2):
                            pe.wait_ge(hot_ready, 2 * j + (h + 1))
                            if not wide:
                                pe.wait_ge(gathered[h], 16 * HALF * j + 16 * HALF)
                            for u in range(HALF):
                                tile = j * CHUNKS + (h * HALF + u)
                                if wide:
                                    pe.wait_ge(w_ready, tile + 1)
                                    pe.wait_ge(part_added, tile + 7)
                                    w = W[:, u % 4, :]
                                    for q in range(4):
                                        pe.matmul(acc[:, u % 2, P * q:P * q + P], w[:, P * q:P * q + P],
                                                  hot[:, h, u, :], start=True, stop=True)
                                    pe.matmul(acc_b[:, u % 2, 0:P], w[:, 4 * P:4 * P + D], hot[:, h, u, :],
                                              start=True, stop=True).then_inc(part_ready, 1)
                                else:
                                    if u % 4 == 0:
                                        pe.wait_ge(part_added, tile + 4)
                                    last = pe.matmul(acc[0:D, u // 4, P * (u % 4):P * (u % 4) + P],
                                                     xs[:, h, D * u:D * u + D], hot[:, h, u, :],
                                                     start=True, stop=True)
                                    if u % 4 == 3:
                                        last.then_inc(part_ready, 4)

                @block.vector
                def _(dve):
                    link(dve, dve.memset(sums[:, :, :], 0.0))
                    link(dve, dve.memset(sums_b[:, :], 0.0))
                    dve.sem_inc(part_added, 8)

                    def weigh(j, h, u):
                        tile = j * CHUNKS + (h * HALF + u)
                        dve.wait_ge(part_ready, tile + 13)
                        dve.tensor_tensor(
                            W[:, u % 4, :].rearrange("p (k f) -> p k f", f=D),
                            fac[:, bass.ds(tile, 1), :].rearrange("p o k -> p (o k)").unsqueeze(2).to_broadcast([P, NF, D]),
                            xs[:, h, D * u:D * u + D].unsqueeze(1).to_broadcast([P, NF, D]),
                            ALU.mult).then_inc(w_ready, 1)

                    def add(j, h, u, base):
                        tile = j * CHUNKS + (h * HALF + u)
                        dve.wait_ge(part_ready, tile + 17)
                        dve.wait_ge(part_added, tile + 8)
                        if wide:
                            at = sums[:, :, bass.ds(base, P)]
                            dve.tensor_tensor(at, at, acc[:, u % 2, :].rearrange("p (q n) -> p q n", q=4), ALU.add)
                            at = sums_b[:, bass.ds(base, P)]
                            dve.tensor_tensor(at, at, acc_b[:, u % 2, 0:P], ALU.add).then_inc(part_added, 1)
                        else:
                            at = sums[0:D, 0, bass.ds(base, P)]
                            dve.tensor_tensor(at, at, acc[0:D, u // 4, P * (u % 4):P * (u % 4) + P], ALU.add
                                              ).then_inc(part_added, 1)

                    with dve.Fori(0, TPC) as j:
                        for h in range(2):
                            bases = window_starts(dve, base_of, j, h)
                            dve.wait_ge(part_ready, 16 * j + (8 * h + 8))
                            dve.tensor_tensor(
                                hot[:, h, :, :], iota[:, :].unsqueeze(1).to_broadcast([P, HALF, P]),
                                window_of[:, bass.ds(j * CHUNKS + h * HALF, HALF)].unsqueeze(2).to_broadcast([P, HALF, P]),
                                ALU.is_equal).then_inc(hot_ready, 1)
                            if wide:
                                dve.wait_ge(gathered[h], 16 * HALF * j + 16 * HALF)
                                weigh(j, h, 0)
                            for u in range(HALF):
                                if wide and u + 1 < HALF:
                                    weigh(j, h, u + 1)
                                add(j, h, u, bases[u])

        update_block(-1)
        for stage in range(3):
            aggregate(stage)
            update_block(stage)
            if stop == f"agg{stage}":
                dump = Count(sem("dump"))
                with nc.Block() as block:
                    @block.sync
                    def _(sp):
                        dump.by(sp.dma_start(out["o_x"], x_sb[:, :, :]), 16)
                        dump.by(sp.dma_start(out["o_h"], h_sb[:, :, :]), 16)
                        sp.wait_ge(dump.sem, dump.n)
                return nc
        rec_stack.close()

        same = sb(top, "same", [P, CLEN + 1], BF16)
        same_neg = sb(top, "same_neg", [P, CLEN + 1], BF16)
        head_is = [sb(top, f"edge_seg{k}", [P, CLEN], BF16) for k in range(2)]
        head_neg = [sb(top, f"edge_neg{k}", [P, CLEN], BF16) for k in range(2)]
        cross = sb(top, "cross", [P, 2, 2, P])
        cross_neg = sb(top, "cross_neg", [P, 2, 2, P])
        slopes = sb(top, "slopes", [P, LAYERS])
        with ExitStack() as st:
            rows = sb(st, "rows", [P, CLEN])
            same_head = sb(st, "same_head", [P, P])
            ends = ps(st, "ends", [P, 2, P])
            rows_loaded = sem("rows_loaded")
            ends_ready = sem("ends_ready")
            with nc.Block() as block:

                @block.sync
                def _(sp):
                    sp.dma_start(same_head[:, :], a["c_same_head"]).then_inc(rows_loaded, 16)
                    by_chunk = dst_rows[0:TILES, :].rearrange("(j c) e -> c j e", c=CHUNKS)
                    for h in range(HEADS):
                        sp.dma_start(rows[h:P:HEADS, :].rearrange("c (j e) -> c j e", e=P), by_chunk
                                     ).then_inc(rows_loaded, 16)
                    sp.wait_ge(rows_loaded, 16 * (HEADS + 1))

                @block.vector
                def _(dve):
                    for k in range(LAYERS):
                        link(dve, dve.memset(slopes[:, k:k + 1], 0.01 if k < LAYERS - 1 else 1.0))
                    link(dve, dve.memset(same[:, :], 0.0))
                    dve.wait_ge(rows_loaded, 16 * (HEADS + 1))
                    link(dve, dve.tensor_tensor(same[:, 1:CLEN], rows[:, 1:CLEN], rows[:, 0:CLEN - 1], ALU.is_equal))
                    link(dve, dve.tensor_scalar(same_neg[:, :], same[:, :], -1.0, BIG, ALU.add, ALU.mult))
                    for k in range(2):
                        mine = rows[:, 0:1] if k == 0 else rows[:, CLEN - 1:CLEN]
                        link(dve, dve.tensor_scalar(head_is[k][:, :], rows[:, :], mine, None, ALU.is_equal))
                        link(dve, dve.tensor_scalar(head_neg[k][:, :], head_is[k][:, :], -1.0, BIG, ALU.add, ALU.mult))
                    dve.wait_ge(ends_ready, 1)
                    for k in range(2):
                        mine = rows[:, 0:1] if k == 0 else rows[:, CLEN - 1:CLEN]
                        for o in range(2):
                            link(dve, dve.tensor_scalar(cross[:, k, o, :], ends[:, o, :], mine, None, ALU.is_equal))
                            link(dve, dve.tensor_tensor(cross[:, k, o, :], cross[:, k, o, :], same_head[:, :], ALU.mult))
                    link(dve, dve.tensor_copy(cross_neg[:, 0, 1, :], ends[:, 1, :]))
                    link(dve, dve.tensor_tensor(cross_neg[:, 0, 0, :], ends[:, 0, :], cross_neg[:, 0, 1, :], ALU.not_equal))
                    for k in range(2):
                        link(dve, dve.tensor_tensor(cross[:, k, 0, :], cross[:, k, 0, :], cross_neg[:, 0, 0, :], ALU.mult))
                    link(dve, dve.tensor_scalar(cross_neg[:, :, :, :], cross[:, :, :, :], -1.0, BIG, ALU.add, ALU.mult))

                @block.tensor
                def _(pe):
                    pe.wait_ge(rows_loaded, 16 * (HEADS + 1))
                    for k in range(2):
                        mine = rows[:, 0:1] if k == 0 else rows[:, CLEN - 1:CLEN]
                        last = pe.matmul(ends[:, k, :], mine.to_broadcast([P, P]), ident[:, :], start=True, stop=True)
                    last.then_inc(ends_ready, 1)

        logits = sb(top, "logits", [P, CLEN])
        w_lr = sb(top, "w_lr", [2 * D, HEADS * D])
        w_out = sb(top, "w_out", [P, 2, D])
        att_z = sb(top, "att_z", [P, 2, 2 * P - HEADS])
        bgb = sb(top, "bgb", [NP5, 3, D])

        names = ("weights", "idx_ready", "st_ready", "xt_ready", "xt_out", "z_ready", "relu_done", "leaky", "scored", "lg_out",
                 "chain", "act_done", "pe_done", "al_staged", "al_turned", "al_ready", "hot_ready", "w_ready",
                 "part_ready", "part_added", "products", "stored", "att_zeroed", "y_ready", "colsum")
        s = {n: sem("l_" + n) for n in names}
        loaded1 = [sem(f"l_loaded1{h}") for h in range(2)]
        loaded2 = [sem(f"l_loaded2{h}") for h in range(2)]
        xs_stored = [sem(f"l_xs_stored{h}") for h in range(2)]
        gathered = [sem(f"l_gathered{h}") for h in range(2)]

        with nc.Fori(0, LAYERS) as layer:
            lchain, lact, lpe = Count(s["chain"]), Count(s["act_done"]), Count(s["pe_done"])

            def step(dve, instruction):
                dve.wait_ge(lchain.sem, lchain.by(instruction))

            with ExitStack() as st, nc.Block() as block:
                xs = sb(st, "xs", [P, 2, HALF * D])
                idx = sb(st, "idx", [P, 2, HALF], I32)
                xwin = sb(st, "xwin", [P, 2, HALF, D])
                locb = sb(st, "locb", [P, 2, HALF * P])
                hot_t = sb(st, "hot_t", [P, 2, HALF * P])
                xz = sb(st, "xz", [2 * D, 2, 512])
                act_z = sb(st, "act_z", [P, 2, 2, 512])
                xt = ps(st, "xt", [2 * D, 2, 512])
                z = ps(st, "z", [P, 2, 2, 512])
                lg = ps(st, "lg", [P, 512])

                @block.sync
                def _(sp):
                    one = bass.ds(layer, 1)
                    wl = a["Wl"][one, :, :].rearrange("o f n -> (o f) n")
                    sp.dma_start(w_lr[0:D, :], wl).then_inc(s["weights"], 16)
                    sp.dma_start(w_lr[D:2 * D, :], a["Wr"][one, :, :].rearrange("o f n -> (o f) n")
                                 ).then_inc(s["weights"], 16)
                    for h in range(HEADS):
                        sp.dma_start(w_out[D * (h % 4):D * (h % 4) + D, h // 4, :], wl[:, D * h:D * h + D]
                                     ).then_inc(s["weights"], 16)
                    sp.dma_start(bgb[:, :, :], a["bgb"][one, :, :].to_broadcast([NP5, 3, D])
                                 ).then_inc(s["weights"], 16)
                    sp.wait_ge(s["att_zeroed"], 1)
                    for h in range(HEADS):
                        col = P - HEADS + h
                        sp.dma_start(att_z[D * (h % 4):D * (h % 4) + D, h // 4, col:col + 1],
                                     a["att"][one, h, :].rearrange("o c -> c o")).then_inc(s["weights"], 16)
                    with sp.Fori(0, TPC) as j:
                        for h in range(2):
                            slot = j * CHUNKS + h * HALF
                            sp.wait_ge(s["xt_ready"], 4 * j + (2 * h + 2))
                            starts = window_starts(sp, base_i, j, h)
                            for u in range(HALF):
                                sp.dma_start(xwin[:, h, u, :], htab[bass.ds(starts[u], P), :]).then_inc(loaded1[h], 16)
                            sp.dma_start(locb[:, h, :],
                                         loc_rows[bass.ds(slot, HALF), :].rearrange("(o t) e -> o (t e)", o=1
                                                                                    ).to_broadcast([P, HALF * P])
                                         ).then_inc(loaded1[h], 16)
                        for h in range(2):
                            sp.wait_ge(gathered[h], layer * (16 * HALF * TPC) + j * (16 * HALF) + 16 * HALF)
                            sp.dma_start(xs_dram[:, bass.ds((j * CHUNKS + h * HALF) * D, HALF * D)], xs[:, h, :]
                                         ).then_inc(xs_stored[h], 16)
                    for h in range(2):
                        sp.wait_ge(xs_stored[h], 16 * TPC)

                @block.gpsimd
                def _(pool):
                    with pool.Fori(0, TPC) as j:
                        for h in range(2):
                            pool.wait_ge(s["idx_ready"], 2 * j + (h + 1))
                            pool.sem_inc(pool_turns, 1)
                            for u in range(HALF):
                                pool.indirect_dma_start(
                                    out=xs[:, h, D * u:D * u + D], out_offset=None, in_=htab,
                                    in_offset=bass.IndirectOffsetOnAxis(ap=idx[:, h, u:u + 1], axis=0)
                                ).then_inc(gathered[h], 16)

                @block.scalar
                def _(act):
                    for h in range(2):
                        act.activation(idx[:, h, :], src_all[:, HALF * h:HALF * h + HALF], ACT.Copy
                                       ).then_inc(s["idx_ready"], 1)
                    act.sem_inc(s["xt_out"], 2)
                    act.sem_inc(s["lg_out"], 1)

                    def relu(j, q):
                        act.wait_ge(s["z_ready"], 4 * j + (q + 3))
                        act.wait_ge(s["scored"], 4 * j + (q + 1))
                        for k in range(2):
                            last = act.activation(act_z[:, q % 2, k, :], z[:, q % 2, k, :], ACT.Relu, scale=0.8)
                        last.then_inc(s["relu_done"], 1)

                    with act.Fori(0, TPC) as j:
                        for q in range(5):
                            if q < 4:
                                act.wait_ge(s["xt_ready"], 4 * j + (q + 5))
                                act.wait_ge(s["z_ready"], 4 * j + (q + 1))
                                act.activation(xz[:, q % 2, :], xt[:, q % 2, :], ACT.Copy).then_inc(s["xt_out"], 1)
                            if q in (1, 3):
                                h = q // 2
                                act.wait_ge(xs_stored[h], 16 * j + 16)
                                act.activation(idx[:, h, :],
                                               src_all[:, bass.ds(j * CHUNKS + (CHUNKS + h * HALF), HALF)], ACT.Copy
                                               ).then_inc(s["idx_ready"], 1)
                            if q in (1, 2, 3, 4):
                                relu(j, q - 1)
                        act.wait_ge(s["scored"], 4 * j + 6)
                        act.activation(logits[:, bass.ds(j * P, P)], lg[:, 0:P], ACT.Copy).then_inc(s["lg_out"], 1)

                @block.vector
                def _(dve):
                    dve.memset(att_z[:, :, :], 0.0).then_inc(s["att_zeroed"], 1)
                    dve.sem_inc(s["st_ready"], 2)
                    dve.sem_inc(s["leaky"], 2)

                    def leaky(j, q):
                        dve.wait_ge(s["relu_done"], 4 * j + (q + 1))
                        for k in range(2):
                            last = dve.scalar_tensor_tensor(act_z[:, q % 2, k, :], z[:, q % 2, k, :], 0.2,
                                                            act_z[:, q % 2, k, :], ALU.mult, ALU.add)
                        last.then_inc(s["leaky"], 1)

                    with dve.Fori(0, TPC) as j:
                        for h in range(2):
                            dve.wait_ge(loaded1[h], (16 * (HALF + 1)) * j + 16 * (HALF + 1))
                            dve.tensor_scalar(hot_t[:, h, :], locb[:, h, :], lanes[:, 0:1], None, ALU.is_equal
                                              ).then_inc(s["st_ready"], 1)
                        for q in range(4):
                            leaky(j, q)

                @block.tensor
                def _(pe):
                    pe.wait_ge(s["weights"], 16 * (2 + 2 * HEADS + 1))
                    pe.sem_inc(s["xt_ready"], 4)
                    pe.sem_inc(s["z_ready"], 2)
                    pe.sem_inc(s["scored"], 2)

                    def turn(j, q):
                        h = q // 2
                        if q % 2 == 0:
                            pe.wait_ge(gathered[h], layer * (16 * HALF * TPC) + j * (16 * HALF) + 16 * HALF)
                            pe.wait_ge(s["st_ready"], 2 * j + (h + 3))
                        pe.wait_ge(s["xt_out"], 4 * j + (q + 1))
                        for u in range(4 * (q % 2), 4 * (q % 2) + 4):
                            cols = slice(P * (u % 4), P * (u % 4) + P)
                            pe.transpose(xt[0:D, q % 2, cols], xs[:, h, D * u:D * u + D], ident[:, :])
                            last = pe.matmul(xt[D:2 * D, q % 2, cols], xwin[:, h, u, :], hot_t[:, h, P * u:P * u + P],
                                             start=True, stop=True)
                        last.then_inc(s["xt_ready"], 1)

                    def project(j, q):
                        pe.wait_ge(s["xt_out"], 4 * j + (q + 3))
                        pe.wait_ge(s["leaky"], 4 * j + (q + 1))
                        for k in range(2):
                            last = pe.matmul(z[:, q % 2, k, :], w_lr[:, P * k:P * k + P], xz[:, q % 2, :],
                                             start=True, stop=True)
                        last.then_inc(s["z_ready"], 1)

                    def score(j, q):
                        pe.wait_ge(s["leaky"], 4 * j + (q + 3))
                        if q == 0:
                            pe.wait_ge(s["lg_out"], j + 1)
                        for u in range(4):
                            at = P - HEADS - HEADS * (4 * q + u)
                            for k in range(2):
                                last = pe.matmul(lg[:, 0:P], att_z[:, k, at:at + P],
                                                 act_z[:, q % 2, k, P * u:P * u + P],
                                                 start=(q == 0 and u == 0 and k == 0),
                                                 stop=(q == 3 and u == 3 and k == 1))
                        last.then_inc(s["scored"], 1)

                    with pe.Fori(0, TPC) as j:
                        turn(j, 0)
                        turn(j, 1)
                        project(j, 0)
                        turn(j, 2)
                        project(j, 1)
                        score(j, 0)
                        turn(j, 3)
                        project(j, 2)
                        score(j, 1)
                        project(j, 3)
                        score(j, 2)
                        score(j, 3)

            with ExitStack() as st, nc.Block() as block:
                fwd = sb(st, "fwd", [P, CLEN])
                tot = sb(st, "tot", [P, CLEN])
                mixed = sb(st, "mixed", [P, 2, P])
                mine = sb(st, "mine", [P, 2])
                other = ps(st, "other", [P, 2, P])
                p_ready, to_exp = [], []

                def segment_total(dve, values, is_max, round_):
                    keep = same_neg if is_max else same
                    op0, op1 = (ALU.add, ALU.max) if is_max else (ALU.mult, ALU.add)
                    start = -BIG if is_max else 0.0
                    step(dve, dve.tensor_tensor_scan(fwd[:, :], keep[:, 0:CLEN], values, start, op0, op1))
                    step(dve, dve.tensor_tensor_scan(tot[:, ::-1], keep[:, CLEN:0:-1], fwd[:, ::-1], start,
                                                     op0, ALU.max))
                    dve.sem_inc(s["y_ready"], 1)
                    dve.wait_ge(s["pe_done"], round_)
                    for k in range(2):
                        step(dve, dve.tensor_tensor(mixed[:, :, :], other[:, :, :],
                                                    (cross_neg if is_max else cross)[:, k, :, :],
                                                    ALU.add if is_max else ALU.mult))
                        step(dve, (dve.reduce_max if is_max else dve.reduce_sum)(
                            mine[:, k:k + 1], mixed[:, :, :].rearrange("p o n -> p (o n)"), AX_X))
                    for k in range(2):
                        step(dve, dve.scalar_tensor_tensor(
                            tot[:, :], (head_neg if is_max else head_is)[k][:, :], mine[:, k:k + 1], tot[:, :],
                            ALU.add if is_max else ALU.mult, ALU.max))

                @block.vector
                def _(dve):
                    segment_total(dve, logits[:, :], True, 1)
                    step(dve, dve.tensor_tensor(logits[:, :], logits[:, :], tot[:, :], ALU.subtract))
                    dve.sem_inc(s["y_ready"], 1)
                    dve.wait_ge(s["act_done"], 1)
                    segment_total(dve, logits[:, :], False, 2)
                    step(dve, dve.reciprocal(tot[:, :], tot[:, :]))
                    step(dve, dve.tensor_tensor(logits[:, :], logits[:, :], tot[:, :], ALU.mult))

                @block.scalar
                def _(act):
                    act.wait_ge(s["y_ready"], 2)
                    act.activation(logits[:, :], logits[:, :], ACT.Exp).then_inc(s["act_done"], 1)

                @block.tensor
                def _(pe):
                    for round_ in range(2):
                        pe.wait_ge(s["y_ready"], 1 + 2 * round_)
                        for k, col in enumerate((0, CLEN - 1)):
                            last = pe.matmul(other[:, k, :], tot[:, col:col + 1].to_broadcast([P, P]), ident[:, :],
                                             start=True, stop=True)
                        last.then_inc(s["pe_done"], 1)

            with ExitStack() as st:
                sums3 = sb(st, "sums3", [P, 2, WIN])
                with ExitStack() as inner, nc.Block() as block:
                    xs = sb(inner, "xs_again", [P, 2, HALF * D])
                    hot = sb(inner, "hot3", [P, 2, HALF, P])
                    W = sb(inner, "W3", [P, 4, HEADS * D])
                    staged = sb(inner, "staged", [P, P])
                    alpha = sb(inner, "alpha", [P, 2, P // 2])
                    acc = ps(inner, "acc3", [P, 4, 512])
                    al_ps = ps(inner, "al_ps", [P, 512])

                    @block.sync
                    def _(sp):
                        with sp.Fori(0, TPC) as j:
                            for h in range(2):
                                sp.wait_ge(s["part_ready"], 16 * j + (8 * h + 8))
                                sp.dma_start(xs[:, h, :], xs_dram[:, bass.ds((j * CHUNKS + h * HALF) * D, HALF * D)]
                                             ).then_inc(loaded2[h], 16)

                    @block.scalar
                    def _(act):
                        act.sem_inc(s["al_turned"], 1)

                        def stage(j):
                            act.wait_ge(s["al_turned"], j + 1)
                            act.activation(staged[:, :], logits[:, bass.ds(j * P, P)], ACT.Copy
                                           ).then_inc(s["al_staged"], 1)

                        def hand_over(j):
                            for h in range(2):
                                act.wait_ge(s["al_turned"], j + 2)
                                act.wait_ge(s["w_ready"], 16 * j + (8 * h + 8))
                                act.activation(alpha[:, h, :], al_ps[:, P // 2 * h:P // 2 * (h + 1)], ACT.Copy
                                               ).then_inc(s["al_ready"], 1)

                        act.activation(staged[:, :], logits[:, 0:P], ACT.Copy).then_inc(s["al_staged"], 1)
                        with act.Fori(0, TPC - 1) as j:
                            hand_over(j)
                            stage(j + 1)
                        hand_over(TPC - 1)

                    @block.tensor
                    def _(pe):
                        pe.sem_inc(s["part_ready"], 16)

                        def turn(j):
                            pe.wait_ge(s["al_staged"], j + 1)
                            pe.transpose(al_ps[:, 0:P], staged[:, :], ident[:, :]).then_inc(s["al_turned"], 1)

                        def products(j, turn_next):
                            for h in range(2):
                                pe.wait_ge(s["hot_ready"], 2 * j + (h + 1))
                                for u in range(HALF):
                                    tile = j * CHUNKS + (h * HALF + u)
                                    pe.wait_ge(s["w_ready"], tile + 17)
                                    pe.wait_ge(s["part_added"], tile + 5)
                                    for k in range(2):
                                        last = pe.matmul(acc[:, u % 4, P * k:P * k + P], W[:, u % 4, P * k:P * k + P],
                                                         hot[:, h, u, :], start=True, stop=True)
                                    last.then_inc(s["part_ready"], 1)
                                if h == 0 and turn_next:
                                    turn(j + 1)

                        turn(0)
                        with pe.Fori(0, TPC - 1) as j:
                            products(j, True)
                        products(TPC - 1, False)

                    @block.vector
                    def _(dve):
                        step(dve, dve.memset(sums3[:, :, :], 0.0))
                        dve.sem_inc(s["part_added"], 8)
                        dve.sem_inc(s["w_ready"], 16)

                        def weigh(j, h, u):
                            tile = j * CHUNKS + (h * HALF + u)
                            dve.wait_ge(s["part_ready"], tile + 13)
                            dve.tensor_tensor(
                                W[:, u % 4, :].rearrange("p (k f) -> p k f", f=D),
                                alpha[:, h, HEADS * u:HEADS * (u + 1)].unsqueeze(2
                                    ).to_broadcast([P, HEADS, D]),
                                xs[:, h, D * u:D * u + D].unsqueeze(1).to_broadcast([P, HEADS, D]),
                                ALU.mult).then_inc(s["w_ready"], 1)

                        def add(j, h, u, base):
                            tile = j * CHUNKS + (h * HALF + u)
                            dve.wait_ge(s["part_ready"], tile + 17)
                            dve.wait_ge(s["part_added"], tile + 8)
                            at = sums3[:, :, bass.ds(base, P)]
                            dve.tensor_tensor(at, at, acc[:, u % 4, 0:2 * P].rearrange("p (k n) -> p k n", k=2),
                                              ALU.add).then_inc(s["part_added"], 1)

                        def open_half(j, h):
                            dve.wait_ge(s["part_ready"], 16 * j + (8 * h + 8))
                            dve.tensor_tensor(
                                hot[:, h, :, :], iota[:, :].unsqueeze(1).to_broadcast([P, HALF, P]),
                                loc_full[:, bass.ds(j * CHUNKS + h * HALF, HALF)].unsqueeze(2
                                    ).to_broadcast([P, HALF, P]),
                                ALU.is_equal).then_inc(s["hot_ready"], 1)
                            dve.wait_ge(loaded2[h], 16 * j + 16)
                            dve.wait_ge(s["al_ready"], 2 * j + (h + 1))

                        def round_(j, more):
                            for t in range(CHUNKS):
                                h, u = divmod(t, HALF)
                                if u == 0:
                                    bases = window_starts(dve, base_i, j, h)
                                ahead = t + LAG
                                if ahead < CHUNKS or more:
                                    ja, (ha, ua) = j + ahead // CHUNKS, divmod(ahead % CHUNKS, HALF)
                                    if ua == 0:
                                        open_half(ja, ha)
                                    weigh(ja, ha, ua)
                                add(j, h, u, bases[u])

                        open_half(0, 0)
                        for u in range(LAG):
                            weigh(0, 0, u)
                        with dve.Fori(0, TPC - 1) as j:
                            round_(j, True)
                        round_(TPC - 1, False)

                with ExitStack() as inner, nc.Block() as block:
                    prod = ps(inner, "prod3", [P, 2, 512])
                    colsum = ps(inner, "colsum", [P, 512])
                    y = sb(inner, "y", [NP5, NT5, D])
                    part = sb(inner, "part", [NP5, D])
                    moment = sb(inner, "moment", [NP5, 2, D])
                    base_act = 1

                    @block.tensor
                    def _(pe):
                        for t in range(NT5):
                            got = prod[0:NP5, t // 16, D * (t % 16):D * (t % 16) + D]
                            cols = slice(t, t + NT5 * (NP5 - 1) + 1, NT5)
                            for k in range(2):
                                last = pe.matmul(got, sums3[:, k, cols], w_out[:, k, :], start=(k == 0), stop=(k == 1))
                        last.then_inc(s["products"], 1)
                        for k in range(2):
                            pe.wait_ge(s["colsum"], 2 * k + 1)
                            pe.matmul(colsum[0:NP5, D * k:D * k + D], ones[0:NP5, 0:NP5], part[:, :],
                                      start=True, stop=True).then_inc(s["colsum"], 1)

                    @block.vector
                    def _(dve):
                        dve.wait_ge(s["products"], 1)
                        for k, (lo, hi) in enumerate(((0, 16), (16, NT5))):
                            got = prod[0:NP5, k, 0:D * (hi - lo)].rearrange("p (t d) -> p t d", d=D)
                            bias = bgb[:, 0, :].unsqueeze(1).to_broadcast([NP5, hi - lo, D])
                            step(dve, dve.scalar_tensor_tensor(y[:, lo:hi, :], got, 1.0 / HEADS, bias,
                                                               ALU.mult, ALU.add))
                        step(dve, dve.scalar_tensor_tensor(y[:, :, :], y[:, :, :], slopes[0:NP5, bass.ds(layer, 1)],
                                                           y[:, :, :], ALU.mult, ALU.max))
                        step(dve, dve.tensor_tensor(y[:, :, :], y[:, :, :], h_sb[:, :, :], ALU.add))

                        def over_nodes(values, k):
                            step(dve, dve.reduce_sum(part[:, :], values.rearrange("p t d -> p d t"), AX_X))
                            dve.sem_inc(s["colsum"], 1)
                            dve.wait_ge(s["colsum"], 2 * k + 2)
                            step(dve, dve.tensor_scalar(moment[:, k, :], colsum[0:NP5, D * k:D * k + D],
                                                        1.0 / NODES, EPS if k else 0.0, ALU.mult, ALU.add))

                        def by_feature(k_ap):
                            return k_ap.unsqueeze(1).to_broadcast([NP5, NT5, D])

                        over_nodes(y[:, :, :], 0)
                        step(dve, dve.tensor_tensor(y[:, :, :], y[:, :, :], by_feature(moment[:, 0, :]), ALU.subtract))
                        step(dve, dve.tensor_tensor(tmp[:, :, :], y[:, :, :], y[:, :, :], ALU.mult))
                        over_nodes(tmp[:, :, :], 1)
                        dve.sem_inc(s["y_ready"], 1)
                        dve.wait_ge(s["act_done"], 2)
                        step(dve, dve.reciprocal(moment[:, 1, :], moment[:, 1, :]))
                        step(dve, dve.tensor_tensor(moment[:, 1, :], moment[:, 1, :], bgb[:, 1, :], ALU.mult))
                        step(dve, dve.tensor_tensor(y[:, :, :], y[:, :, :], by_feature(moment[:, 1, :]), ALU.mult))
                        step(dve, dve.tensor_tensor(h_sb[:, :, :], y[:, :, :], by_feature(bgb[:, 2, :]), ALU.add))
                        dve.sem_inc(s["y_ready"], 1)

                    @block.scalar
                    def _(act):
                        act.wait_ge(s["y_ready"], 4)
                        act.activation(moment[:, 1, :], moment[:, 1, :], ACT.Sqrt).then_inc(s["act_done"], 1)

                    @block.sync
                    def _(sp):
                        sp.wait_ge(s["y_ready"], 5)
                        sp.dma_start(htab[0:NODES, :].rearrange("(p t) d -> p t d", p=NP5), h_sb[:, :, :]
                                     ).then_inc(s["stored"], 16)
                        sp.wait_ge(s["stored"], 16)

            nc.all_engine_barrier()
            for one in (*s.values(), *loaded1, *loaded2, *xs_stored):
                nc.sync.sem_clear(one)
            nc.all_engine_barrier()

        out_stored = sem("out_stored")
        final_ready = sem("final_ready")
        with nc.Block() as block:

            @block.vector
            def _(dve):
                dve.tensor_tensor(tmp[:, :, :], x_sb[:, :, :], h_sb[:, :, :], ALU.add).then_inc(final_ready, 1)

            @block.sync
            def _(sp):
                sp.wait_ge(final_ready, 1)
                sp.dma_start(out["out"].rearrange("(p t) d -> p t d", p=NP5), tmp[:, :, :]).then_inc(out_stored, 16)
                sp.wait_ge(out_stored, 16)


_PLAIN = ["x", "src", "dst", "edge_attr_16", "L0_gnn_W", "L0_gnn_b", "L1_gnn_kernel", "L1_gnn_bias"]


def shape_constants():
    lane = np.arange(P)
    return {
        "c_ident": np.eye(P, dtype=np.float32),
        "c_iota": np.tile(lane.astype(np.float32), (P, 1)),
        "c_lanes": lane.astype(np.float32)[:, None].copy(),
        "c_tri": (lane[:, None] < lane[None]).astype(np.float32),
        "c_earlier": np.concatenate([np.ones((P, (GC - 1) * NP5)), lane[:, None] > lane[None, :NP5]],
                                    axis=1).astype(np.float32),
        "c_node": (np.arange(SELF_CALLS)[None] * P + lane[:, None]).astype(np.float32),
        "c_same_head": (lane[:, None] % HEADS == lane[None] % HEADS).astype(np.float32),
    }


def kernel(**inputs):
    import concourse.bacc as _bacc
    from concourse.bass_utils import run_bass_kernel_spmd as _run

    nc = _bacc.Bacc("TRN2", target_bir_lowering=False, num_devices=1)
    arrays = {n: np.ascontiguousarray(inputs[n]) for n in _PLAIN}
    for short in ("Wl", "Wr", "att"):
        arrays[short] = np.stack([np.asarray(inputs[f"L3_gnn_{short}{k}"]) for k in (1, 2, 3)])
    arrays["bgb"] = np.stack([np.stack([np.asarray(inputs[f"L3_gnn_{n}{k}"]) for n in ("b", "g", "be")])
                              for k in (1, 2, 3)])
    arrays.update(shape_constants())
    arrays = {f"in_{n}_dram": v for n, v in arrays.items()}
    args = {n[3:-5]: nc.dram_tensor(n, v.shape, mybir.dt.from_np(v.dtype), kind="ExternalInput").ap()
            for n, v in arrays.items()}
    out = {"out": nc.dram_tensor("out_0_dram", (NODES, D), F32, kind="ExternalOutput").ap()}
    build(nc, args, out)
    r = _run(nc, [arrays], core_ids=[0])
    return r.results[0]["out_0_dram"]
```
